# Optimizing a Trainium2 kernel written in Bass

```python
import numpy as np
import jax
import jax.numpy as jnp

def _softmax(x, axis=-1):
    return jax.nn.softmax(x, axis=axis)

def _gelu(x):
    return jax.nn.gelu(x, approximate=True)

def _silu(x):
    return jax.nn.silu(x)

def _sigmoid(x):
    return jax.nn.sigmoid(x)

def _layernorm(x, axis=-1, eps=1e-05):
    m = jnp.mean(x, axis=axis, keepdims=True)
    v = jnp.var(x, axis=axis, keepdims=True)
    return (x - m) / jnp.sqrt(v + eps)

def _scatter_add(tgt, idx, src, axis=0):
    return tgt.at[idx].add(src)

def _segment_sum(src, seg, n):
    return jax.ops.segment_sum(src, seg, n)
kernel_name = 'mk_dlrm_tower_d1_rec_r8_343027'

def setup_inputs(seed: int=0):
    np.random.seed(seed)
    _w = jnp.asarray

    def _rec_inputs():
        import jax
        import jax.numpy as jnp
        _tk = jax.random.key(seed)
        dense_ctx = jax.random.normal(jax.random.fold_in(_tk, 190), (2048, 16), jnp.float32)
        ids = jnp.stack([jax.random.randint(jax.random.fold_in(_tk, 200 + f), (2048,), 0, v, jnp.int32) for f, v in enumerate([1000, 1000, 1000, 1250, 1250, 1250, 1250, 1000, 12500, 125000, 1250, 1250, 1000, 1000, 12500, 125000, 1250, 125000, 1250, 12500, 1250, 12500, 12500, 1250, 1000, 1250, 1000, 1250, 1250, 12500, 1250, 1250])], axis=1)
        tbl_0 = 0.05 * jax.random.normal(jax.random.fold_in(_tk, 500 + 0), (1000, 64), jnp.float32)
        tbl_1 = 0.05 * jax.random.normal(jax.random.fold_in(_tk, 500 + 1), (1000, 64), jnp.float32)
        tbl_2 = 0.05 * jax.random.normal(jax.random.fold_in(_tk, 500 + 2), (1000, 64), jnp.float32)
        tbl_3 = 0.05 * jax.random.normal(jax.random.fold_in(_tk, 500 + 3), (1250, 64), jnp.float32)
        tbl_4 = 0.05 * jax.random.normal(jax.random.fold_in(_tk, 500 + 4), (1250, 64), jnp.float32)
        tbl_5 = 0.05 * jax.random.normal(jax.random.fold_in(_tk, 500 + 5), (1250, 64), jnp.float32)
        tbl_6 = 0.05 * jax.random.normal(jax.random.fold_in(_tk, 500 + 6), (1250, 64), jnp.float32)
        tbl_7 = 0.05 * jax.random.normal(jax.random.fold_in(_tk, 500 + 7), (1000, 64), jnp.float32)
        tbl_8 = 0.05 * jax.random.normal(jax.random.fold_in(_tk, 500 + 8), (12500, 64), jnp.float32)
        tbl_9 = 0.05 * jax.random.normal(jax.random.fold_in(_tk, 500 + 9), (125000, 64), jnp.float32)
        tbl_10 = 0.05 * jax.random.normal(jax.random.fold_in(_tk, 500 + 10), (1250, 64), jnp.float32)
        tbl_11 = 0.05 * jax.random.normal(jax.random.fold_in(_tk, 500 + 11), (1250, 64), jnp.float32)
        tbl_12 = 0.05 * jax.random.normal(jax.random.fold_in(_tk, 500 + 12), (1000, 64), jnp.float32)
        tbl_13 = 0.05 * jax.random.normal(jax.random.fold_in(_tk, 500 + 13), (1000, 64), jnp.float32)
        tbl_14 = 0.05 * jax.random.normal(jax.random.fold_in(_tk, 500 + 14), (12500, 64), jnp.float32)
        tbl_15 = 0.05 * jax.random.normal(jax.random.fold_in(_tk, 500 + 15), (125000, 64), jnp.float32)
        tbl_16 = 0.05 * jax.random.normal(jax.random.fold_in(_tk, 500 + 16), (1250, 64), jnp.float32)
        tbl_17 = 0.05 * jax.random.normal(jax.random.fold_in(_tk, 500 + 17), (125000, 64), jnp.float32)
        tbl_18 = 0.05 * jax.random.normal(jax.random.fold_in(_tk, 500 + 18), (1250, 64), jnp.float32)
        tbl_19 = 0.05 * jax.random.normal(jax.random.fold_in(_tk, 500 + 19), (12500, 64), jnp.float32)
        tbl_20 = 0.05 * jax.random.normal(jax.random.fold_in(_tk, 500 + 20), (1250, 64), jnp.float32)
        tbl_21 = 0.05 * jax.random.normal(jax.random.fold_in(_tk, 500 + 21), (12500, 64), jnp.float32)
        tbl_22 = 0.05 * jax.random.normal(jax.random.fold_in(_tk, 500 + 22), (12500, 64), jnp.float32)
        tbl_23 = 0.05 * jax.random.normal(jax.random.fold_in(_tk, 500 + 23), (1250, 64), jnp.float32)
        tbl_24 = 0.05 * jax.random.normal(jax.random.fold_in(_tk, 500 + 24), (1000, 64), jnp.float32)
        tbl_25 = 0.05 * jax.random.normal(jax.random.fold_in(_tk, 500 + 25), (1250, 64), jnp.float32)
        tbl_26 = 0.05 * jax.random.normal(jax.random.fold_in(_tk, 500 + 26), (1000, 64), jnp.float32)
        tbl_27 = 0.05 * jax.random.normal(jax.random.fold_in(_tk, 500 + 27), (1250, 64), jnp.float32)
        tbl_28 = 0.05 * jax.random.normal(jax.random.fold_in(_tk, 500 + 28), (1250, 64), jnp.float32)
        tbl_29 = 0.05 * jax.random.normal(jax.random.fold_in(_tk, 500 + 29), (12500, 64), jnp.float32)
        tbl_30 = 0.05 * jax.random.normal(jax.random.fold_in(_tk, 500 + 30), (1250, 64), jnp.float32)
        tbl_31 = 0.05 * jax.random.normal(jax.random.fold_in(_tk, 500 + 31), (1250, 64), jnp.float32)
        _rk = jax.random.fold_in(_tk, 7)
        W_top1 = 0.0441942 * jax.random.normal(jax.random.fold_in(_tk, 801), (512, 512), jnp.float32)
        W_top2 = 0.0441942 * jax.random.normal(jax.random.fold_in(_tk, 802), (512, 256), jnp.float32)
        W_top3 = 0.0625 * jax.random.normal(jax.random.fold_in(_tk, 803), (256, 1), jnp.float32)
        b_top1 = jnp.zeros((512,), jnp.float32)
        b_top2 = jnp.zeros((256,), jnp.float32)
        return (dense_ctx, ids, tbl_0, tbl_1, tbl_2, tbl_3, tbl_4, tbl_5, tbl_6, tbl_7, tbl_8, tbl_9, tbl_10, tbl_11, tbl_12, tbl_13, tbl_14, tbl_15, tbl_16, tbl_17, tbl_18, tbl_19, tbl_20, tbl_21, tbl_22, tbl_23, tbl_24, tbl_25, tbl_26, tbl_27, tbl_28, tbl_29, tbl_30, tbl_31, W_top1, b_top1, W_top2, b_top2, W_top3)
    dense_ctx, ids, tbl_0, tbl_1, tbl_2, tbl_3, tbl_4, tbl_5, tbl_6, tbl_7, tbl_8, tbl_9, tbl_10, tbl_11, tbl_12, tbl_13, tbl_14, tbl_15, tbl_16, tbl_17, tbl_18, tbl_19, tbl_20, tbl_21, tbl_22, tbl_23, tbl_24, tbl_25, tbl_26, tbl_27, tbl_28, tbl_29, tbl_30, tbl_31, W_top1, b_top1, W_top2, b_top2, W_top3 = _rec_inputs()

    def _L0_rec_setup():
        import jax, jax.numpy as jnp
        import numpy as np
        BATCH = 1024
        NUM_FIELDS = 32
        EMBED_DIM = 64
        NUM_IX = NUM_FIELDS * (NUM_FIELDS - 1) // 2
        key = jax.random.key(seed)
        kx, kk = jax.random.split(key)
        x = jax.random.normal(kx, (BATCH, NUM_FIELDS, EMBED_DIM), dtype=jnp.float32)
        fan = EMBED_DIM + EMBED_DIM
        limit = float(np.sqrt(6.0 / fan))
        kernel = jax.random.uniform(kk, (EMBED_DIM, NUM_IX, EMBED_DIM), dtype=jnp.float32, minval=-limit, maxval=limit)
        return {'x': x, 'kernel': kernel}
    _L0_rec_all = _L0_rec_setup()
    _L0_rec_in = {k: v for k, v in _L0_rec_all.items() if k in ('kernel',)}
    del _L0_rec_all
    return {'dense_ctx': dense_ctx, 'ids': ids, 'tbl_0': tbl_0, 'tbl_1': tbl_1, 'tbl_2': tbl_2, 'tbl_3': tbl_3, 'tbl_4': tbl_4, 'tbl_5': tbl_5, 'tbl_6': tbl_6, 'tbl_7': tbl_7, 'tbl_8': tbl_8, 'tbl_9': tbl_9, 'tbl_10': tbl_10, 'tbl_11': tbl_11, 'tbl_12': tbl_12, 'tbl_13': tbl_13, 'tbl_14': tbl_14, 'tbl_15': tbl_15, 'tbl_16': tbl_16, 'tbl_17': tbl_17, 'tbl_18': tbl_18, 'tbl_19': tbl_19, 'tbl_20': tbl_20, 'tbl_21': tbl_21, 'tbl_22': tbl_22, 'tbl_23': tbl_23, 'tbl_24': tbl_24, 'tbl_25': tbl_25, 'tbl_26': tbl_26, 'tbl_27': tbl_27, 'tbl_28': tbl_28, 'tbl_29': tbl_29, 'tbl_30': tbl_30, 'tbl_31': tbl_31, 'W_top1': W_top1, 'b_top1': b_top1, 'W_top2': W_top2, 'b_top2': b_top2, 'W_top3': W_top3, 'L0_rec_kernel': _L0_rec_in['kernel']}

def reference(dense_ctx, ids, tbl_0, tbl_1, tbl_2, tbl_3, tbl_4, tbl_5, tbl_6, tbl_7, tbl_8, tbl_9, tbl_10, tbl_11, tbl_12, tbl_13, tbl_14, tbl_15, tbl_16, tbl_17, tbl_18, tbl_19, tbl_20, tbl_21, tbl_22, tbl_23, tbl_24, tbl_25, tbl_26, tbl_27, tbl_28, tbl_29, tbl_30, tbl_31, W_top1, b_top1, W_top2, b_top2, W_top3, L0_rec_kernel):
    import jax
    import jax.numpy as jnp

    def _L0_rec_ref(x, kernel):
        import jax, jax.numpy as jnp
        import numpy as np
        BATCH = 1024
        NUM_FIELDS = 32
        EMBED_DIM = 64
        NUM_IX = NUM_FIELDS * (NUM_FIELDS - 1) // 2
        num_fields = x.shape[1]
        row, col = np.triu_indices(num_fields, k=1)
        p = x[:, row]
        q = x[:, col]
        out = jnp.einsum('bni,oni,bno->bn', p, kernel, q)
        return out
    e = jnp.stack([tbl_0[ids[:, 0]], tbl_1[ids[:, 1]], tbl_2[ids[:, 2]], tbl_3[ids[:, 3]], tbl_4[ids[:, 4]], tbl_5[ids[:, 5]], tbl_6[ids[:, 6]], tbl_7[ids[:, 7]], tbl_8[ids[:, 8]], tbl_9[ids[:, 9]], tbl_10[ids[:, 10]], tbl_11[ids[:, 11]], tbl_12[ids[:, 12]], tbl_13[ids[:, 13]], tbl_14[ids[:, 14]], tbl_15[ids[:, 15]], tbl_16[ids[:, 16]], tbl_17[ids[:, 17]], tbl_18[ids[:, 18]], tbl_19[ids[:, 19]], tbl_20[ids[:, 20]], tbl_21[ids[:, 21]], tbl_22[ids[:, 22]], tbl_23[ids[:, 23]], tbl_24[ids[:, 24]], tbl_25[ids[:, 25]], tbl_26[ids[:, 26]], tbl_27[ids[:, 27]], tbl_28[ids[:, 28]], tbl_29[ids[:, 29]], tbl_30[ids[:, 30]], tbl_31[ids[:, 31]]], axis=1)
    z = _L0_rec_ref(e, L0_rec_kernel)
    z = z.reshape(z.shape[0], -1)
    h = jnp.concatenate([z, dense_ctx], axis=1)
    h = jnp.maximum(h @ W_top1 + b_top1, 0.0)
    h = jnp.maximum(h @ W_top2 + b_top2, 0.0)
    y = h @ W_top3
    return y

_drawn_inputs = setup_inputs


def setup_inputs(seed=0):
    import zlib

    import numpy as np

    out = dict(_drawn_inputs(seed))
    spreads = {'b_top1': (0.0, 0.1), 'b_top2': (0.0, 0.1)}
    factors = {}
    for name, (base, spread) in spreads.items():
        noise = np.random.default_rng([zlib.crc32(name.encode()), seed]).standard_normal(out[name].shape)
        drawn = base * np.exp(spread * noise) if base else spread * noise
        out[name] = jnp.asarray(drawn.astype(out[name].dtype))
    for name, factor in factors.items():
        out[name] = (out[name] * factor).astype(out[name].dtype)
    return out
```

```python
import numpy as np
import concourse.bass as bass
import concourse.mybir as mybir
from contextlib import ExitStack

F32 = mybir.dt.float32
F32R = mybir.dt.float32r
I32 = mybir.dt.int32
ALU = mybir.AluOpType
ACT = mybir.ActivationFunctionType

P = 128
B, FIELDS, D = 2048, 32, 64
DENSE = 16
H1, H2 = 512, 256
CHUNK = 512
CHUNKS = B // CHUNK
TILES = CHUNK // P
IDS_HALF = FIELDS // 2

GROUPS = [(j, k) for j in range(1, FIELDS) for k in range((j + 1) // 2)]
NG = len(GROUPS)
PAIRS = NG // 2
QUADS = NG // 4
BLOCKS = 2 * NG // P
QUADS_PER_BLOCK = QUADS // BLOCKS
FIRST = {j: GROUPS.index((j, 0)) for j in range(1, FIELDS)}
LAST = {j: FIRST[j] + (j + 1) // 2 - 1 for j in range(1, FIELDS)}

K_BLOCK = 1024
K_BLOCKS = NG * P // K_BLOCK
LANDING = 8
PRODUCT_SLOTS = 4


def transpose_before_pair(f):
    return 0 if f <= 2 else FIRST[f - 1] // 2 + 1


def z_row(q):
    return P * (q // 64) + 32 * (q % 4) + 2 * (q % 64 // 4)


def build(nc, ids, dense_t, tables, kern, w1, b1, w2, b2, w3, out):
    z_dram = nc.dram_tensor("z_scratch", [CHUNKS, BLOCKS, P, CHUNK], F32, kind="Internal").ap()
    ctx = ExitStack()
    with ctx:
        def sem(name):
            return ctx.enter_context(nc.semaphore(name))

        def sb(name, shape, dt=F32, on=ctx):
            return on.enter_context(nc.sbuf_tensor(name, shape, dt))

        selector = sb("selector", [P, 62])
        identity = sb("identity", [P, P])
        b1_sb = sb("b1_sb", [P, H1 // P])
        b2_sb = sb("b2_sb", [P, H2 // P])
        w3_sb = sb("w3_sb", [P, H2 // P])
        ids_sb = [sb(f"ids_sb{h}", [P, TILES, IDS_HALF], I32) for h in range(2)]

        pair_phase = ExitStack()
        k_split = sb("k_split", [P, NG * P], F32R, pair_phase)
        xt = sb("xt", [P, FIELDS // 2, CHUNK], F32, pair_phase)
        x_hi = sb("x_hi", [P, 2, CHUNK], F32R, pair_phase)
        x_lo = sb("x_lo", [P, 2, CHUNK], F32R, pair_phase)
        landing = sb("landing", [P, LANDING, TILES, D], F32, pair_phase)
        product = sb("product", [P, PRODUCT_SLOTS, 2, CHUNK], F32, pair_phase)
        k_raw = product[:, 0:2].rearrange("p a b n -> p a (b n)")
        doubled = sb("doubled", [P, 2, TILES, 2, D], F32, pair_phase)
        z_stage = sb("z_stage", [P, CHUNK], F32, pair_phase)
        pair_phase.close()

        mlp_phase = ExitStack()
        w1_sb = sb("w1_sb", [P, H1 // P, H1], F32, mlp_phase)
        w2_sb = sb("w2_sb", [P, H1 // P, H2], F32, mlp_phase)
        z_sb = sb("z_sb", [P, CHUNKS, BLOCKS, CHUNK], F32, mlp_phase)
        h1_sb = sb("h1_sb", [P, 2, H1 // P, CHUNK], F32, mlp_phase)
        h2_sb = sb("h2_sb", [P, CHUNKS, H2 // P, CHUNK], F32, mlp_phase)
        y_sb = sb("y_sb", [P, CHUNK], F32, mlp_phase)
        mlp_phase.close()
        mlp_bytes = 4 * (4 * H1 + 4 * H2 + CHUNKS * BLOCKS * CHUNK + 2 * 4 * CHUNK + CHUNKS * 2 * CHUNK + CHUNK)
        mlp_free_pair = -(-mlp_bytes // (4 * P)) // 2 + 1

        t_ps = ctx.enter_context(nc.psum_tensor("t_ps", [P, 2, 2, CHUNK], F32))
        x_ps = ctx.enter_context(nc.psum_tensor("x_ps", [P, 2, CHUNK], F32))
        z_ps = ctx.enter_context(nc.psum_tensor("z_ps", [P, 2, CHUNK], F32))

        ids_loaded = [sem(f"ids_loaded{h}") for h in range(2)]
        gathered = [sem(f"gathered{s}") for s in range(LANDING)]
        doubles_made = sem("doubles_made")
        transposed = sem("transposed")
        lo_made = sem("lo_made")
        xt_copied = sem("xt_copied")
        t_done = sem("t_done")
        products_done = sem("products_done")
        summed = sem("summed")
        z_copied = sem("z_copied")
        z_stored = sem("z_stored")
        k_loaded = [sem(f"k_loaded{s}") for s in range(2)]
        k_rounded = sem("k_rounded")
        k_split_done = sem("k_split_done")
        fields_started = sem("fields_started")
        identity_zeroed = sem("identity_zeroed")
        selector_zeroed = sem("selector_zeroed")
        constants = sem("constants")
        small_loaded = sem("small_loaded")
        w_loaded = sem("w_loaded")
        z_loaded = [sem(f"z_loaded{c}") for c in range(CHUNKS)]
        dense_loaded = [sem(f"dense_loaded{c}") for c in range(CHUNKS)]
        l1_done = sem("l1_done")
        h1_made = sem("h1_made")
        l2_done = sem("l2_done")
        h2_made = sem("h2_made")
        l3_done = sem("l3_done")
        y_made = sem("y_made")
        y_stored = sem("y_stored")

        block = ctx.enter_context(nc.Block())

        @block.sync
        def _(sp):
            def load_ids(c, h):
                rows = ids[bass.ds(c * CHUNK, CHUNK), h * IDS_HALF:(h + 1) * IDS_HALF]
                sp.dma_start(ids_sb[h][:], rows.rearrange("(t p) f -> p t f", p=P)).then_inc(ids_loaded[h], 16)

            load_ids(0, 0)
            load_ids(0, 1)
            for n in range(K_BLOCKS):
                if n >= 2:
                    sp.wait_ge(k_split_done, n - 1)
                for half in range(2):
                    sp.dma_start(k_raw[half * D:(half + 1) * D, n % 2, :],
                                 kern[:, n * K_BLOCK:(n + 1) * K_BLOCK]).then_inc(k_loaded[n % 2], 16)
            sp.dma_start(b1_sb[:], b1.rearrange("(p m) -> p m", p=P)).then_inc(small_loaded, 16)
            sp.dma_start(b2_sb[:], b2.rearrange("(p m) -> p m", p=P)).then_inc(small_loaded, 16)
            sp.dma_start(w3_sb[:], w3.rearrange("(p m) -> p m", p=P)).then_inc(small_loaded, 16)

            def chunk(c, more):
                for b in range(BLOCKS):
                    sp.wait_ge(z_copied, (c + 1) * BLOCKS + b + 1)
                    sp.dma_start(z_dram[bass.ds(c, 1), b].rearrange("a p n -> (a p) n"), z_stage[:])\
                      .then_inc(z_stored, 16)
                    if more and b == 0:
                        sp.wait_ge(transposed, (c + 1) * FIELDS + IDS_HALF)
                        load_ids(c + 1, 0)
                if more:
                    sp.wait_ge(transposed, (c + 2) * FIELDS)
                    load_ids(c + 1, 1)

            with sp.Fori(0, CHUNKS - 1) as c:
                chunk(c, True)

            chunk(CHUNKS - 1, False)
            sp.wait_ge(y_made, CHUNKS)
            sp.dma_start(out.rearrange("(c n) o -> c (n o)", c=CHUNKS), y_sb[0:97:32, :]).then_inc(y_stored, 16)
            sp.wait_ge(y_stored, 16)

        @block.gpsimd
        def _(pool):
            pool.memset(identity[:], 0.0).then_inc(identity_zeroed, 1)
            pool.wait_ge(identity_zeroed, 1)
            pool.affine_select(out=identity[:], in_=identity[:], compare_op=ALU.not_equal, fill=1.0, base=0,
                               pattern=[[-1, P]], channel_multiplier=1).then_inc(constants, 1)
            with pool.Fori(0, CHUNKS) as c:
                for f in range(FIELDS):
                    h, col = f // IDS_HALF, f % IDS_HALF
                    if col == 0:
                        pool.wait_ge(ids_loaded[h], (c + 1) * 16)
                    pool.wait_ge(doubles_made, (c + 1) * FIELDS + f - LANDING + 1)
                    pool.sem_inc(fields_started, 1)
                    for t in range(TILES):
                        pool.indirect_dma_start(
                            out=landing[:, f % LANDING, t, :], out_offset=None, in_=tables[f][:, :],
                            in_offset=bass.IndirectOffsetOnAxis(ap=ids_sb[h][:, t, col:col + 1], axis=0),
                        ).then_inc(gathered[f % LANDING], 16)

            pool.wait_ge(t_done, CHUNKS * PAIRS + mlp_free_pair)
            pool.dma_start(w1_sb[:], w1.rearrange("(k p) n -> p k n", p=P)).then_inc(w_loaded, 16)
            pool.dma_start(w2_sb[:], w2.rearrange("(k p) n -> p k n", p=P)).then_inc(w_loaded, 16)

            def load_z(c):
                pool.wait_ge(z_stored, 16 * BLOCKS * (c + 1))
                pool.dma_start(z_sb[:, c], z_dram[c].rearrange("b p n -> p b n")).then_inc(z_loaded[c], 16)

            def load_dense(c):
                pool.wait_ge(z_loaded[c], 16)
                for m in range(DENSE):
                    row = z_row(LAST[2 * m + 1]) + 1
                    pool.dma_start(z_sb[row % P:row % P + 1, c, row // P, :],
                                 dense_t[m:m + 1, c * CHUNK:(c + 1) * CHUNK]).then_inc(dense_loaded[c], 16)

            for c in range(CHUNKS - 1):
                load_z(c)
            for c in range(CHUNKS - 1):
                load_dense(c)
            load_z(CHUNKS - 1)
            load_dense(CHUNKS - 1)

        @block.tensor
        def _(pe):
            pe.sem_inc(transposed, FIELDS)
            pe.sem_inc(t_done, PAIRS)
            pe.sem_inc(summed, QUADS)
            pe.wait_ge(constants, 3)

            def transpose_field(c, f):
                pe.wait_ge(doubles_made, (c + 1) * FIELDS + f + 1)
                pe.wait_ge(xt_copied, (c + 1) * FIELDS + f - 1)
                pe.wait_ge(lo_made, (c + 1) * (FIELDS - 1) + (f - 2 if f >= 2 else f - 1))
                for t in range(TILES):
                    last = pe.transpose(x_ps[:, f % 2, t * P:(t + 1) * P],
                                        doubled[:, f % 2, t].rearrange("p a d -> p (a d)"), identity[:])
                last.then_inc(transposed, 1)

            def contract_pair(c, p):
                pe.wait_ge(products_done, (c + 1) * PAIRS + p - 1)
                for g in range(2):
                    q = 2 * p + g
                    j, k = GROUPS[q]
                    if k == 0:
                        pe.wait_ge(lo_made, (c + 1) * (FIELDS - 1) + j)
                    if q % (K_BLOCK // P) == 0:
                        pe.wait_ge(k_split_done, q // (K_BLOCK // P) + 1)
                    w = k_split[:, q * P:(q + 1) * P]
                    pe.matmul(t_ps[:, p % 2, g, :], w, x_hi[:, j % 2, :], start=True, stop=False)
                    last = pe.matmul(t_ps[:, p % 2, g, :], w, x_lo[:, j % 2, :], start=False, stop=True)
                last.then_inc(t_done, 1)

            def sum_quad(c, Q):
                b, r = Q // QUADS_PER_BLOCK, Q % QUADS_PER_BLOCK
                if r == 0:
                    pe.wait_ge(z_copied, (c + 1) * BLOCKS + b - 1)
                pe.wait_ge(products_done, (c + 1) * PAIRS + 2 * Q + 2)
                for s in range(4):
                    last = pe.matmul(z_ps[32 * s:32 * s + 32, b % 2, :], selector[:, 30 - 2 * r:62 - 2 * r],
                                     product[:, (2 * Q + s // 2) % PRODUCT_SLOTS, s % 2, :],
                                     start=(r == 0), stop=(r == QUADS_PER_BLOCK - 1), skip_group_check=True)
                last.then_inc(summed, 1)

            with pe.Fori(0, CHUNKS) as c:
                for p in range(PAIRS):
                    for f in range(FIELDS):
                        if transpose_before_pair(f) == p:
                            transpose_field(c, f)
                    contract_pair(c, p)
                    if p % 2 and p > 1:
                        sum_quad(c, p // 2 - 1)
                sum_quad(c, QUADS - 1)

            pe.wait_ge(w_loaded, 32)
            pe.wait_ge(small_loaded, 48)

            def layer1(c):
                pe.wait_ge(z_loaded[c], 16)
                pe.wait_ge(dense_loaded[c], 16 * DENSE)
                for m in range(H1 // P):
                    if c:
                        pe.wait_ge(h1_made, (c - 1) * 4 + m + 1)
                    for k in range(BLOCKS):
                        last = pe.matmul(t_ps[:, m // 2, m % 2, :], w1_sb[:, k, m * P:(m + 1) * P],
                                         z_sb[:, c, k, :], start=(k == 0), stop=(k == BLOCKS - 1))
                    last.then_inc(l1_done, 1)

            def layer2(c):
                pe.wait_ge(h1_made, (c + 1) * 4)
                for m in range(H2 // P):
                    if c:
                        pe.wait_ge(h2_made, (c - 1) * 2 + m + 1)
                    for k in range(H1 // P):
                        last = pe.matmul(x_ps[:, m, :], w2_sb[:, k, m * P:(m + 1) * P],
                                         h1_sb[:, c % 2, k, :], start=(k == 0), stop=(k == H1 // P - 1))
                    last.then_inc(l2_done, 1)

            layer1(0)
            for c in range(CHUNKS):
                if c + 1 < CHUNKS:
                    layer1(c + 1)
                layer2(c)
            pe.wait_ge(h2_made, CHUNKS * 2)
            pe.wait_ge(z_copied, (CHUNKS + 1) * BLOCKS)
            for k in range(H2 // P):
                for c in range(CHUNKS):
                    last = pe.matmul(z_ps[32 * c:32 * c + 1, 0, :], w3_sb[:, k:k + 1], h2_sb[:, c, k, :],
                                     start=(k == 0), stop=(k == H2 // P - 1), skip_group_check=True)
            last.then_inc(l3_done, 1)

        @block.scalar
        def _(act):
            act.sem_inc(doubles_made, FIELDS)
            act.sem_inc(xt_copied, FIELDS)
            act.sem_inc(z_copied, BLOCKS)
            for n in range(K_BLOCKS):
                act.wait_ge(k_loaded[n % 2], 32 * (n // 2 + 1))
                act.activation(k_split[:, n * K_BLOCK:(n + 1) * K_BLOCK], k_raw[:, n % 2, :], ACT.Copy)\
                   .then_inc(k_rounded, 1)

            def double_field(c, f):
                act.wait_ge(gathered[f % LANDING], (c * (FIELDS // LANDING) + f // LANDING + 1) * 16 * TILES)
                act.wait_ge(transposed, (c + 1) * FIELDS + f - 1)
                rows = landing[:, f % LANDING].rearrange("p t (a d) -> p t a d", a=1).to_broadcast((P, TILES, 2, D))
                act.activation(doubled[:, f % 2], rows, ACT.Copy).then_inc(doubles_made, 1)

            def take_field(c, f):
                half = slice(D * (f % 2), D * (f % 2) + D)
                act.wait_ge(transposed, (c + 1) * FIELDS + f + 1)
                if f:
                    if f >= 3:
                        act.wait_ge(t_done, (c + 1) * PAIRS + LAST[f - 2] // 2 + 1)
                    else:
                        act.wait_ge(t_done, c * PAIRS + LAST[f + FIELDS - 2 if f == 1 else FIELDS - 2] // 2 + 1)
                    act.activation(x_hi[:, f % 2, :], x_ps[:, f % 2, :], ACT.Copy)
                act.wait_ge(products_done, c * PAIRS + (FIRST[FIELDS - 1] + f // 2) // 2 + 1)
                act.activation(xt[half, f // 2, :], x_ps[half, f % 2, :], ACT.Copy).then_inc(xt_copied, 1)

            def take_block(c, b):
                act.wait_ge(summed, (c + 1) * QUADS + (b + 1) * QUADS_PER_BLOCK)
                if b:
                    act.wait_ge(z_stored, (c * BLOCKS + b) * 16)
                else:
                    act.wait_ge(z_stored, c * BLOCKS * 16)
                act.activation(z_stage[:], z_ps[:, b % 2, :], ACT.Copy).then_inc(z_copied, 1)

            with act.Fori(0, CHUNKS) as c:
                double_field(c, 0)
                double_field(c, 1)
                for p in range(PAIRS):
                    for f in range(FIELDS):
                        if transpose_before_pair(f) == p:
                            take_field(c, f)
                            if f + 2 < FIELDS:
                                double_field(c, f + 2)
                    if p % (2 * QUADS_PER_BLOCK) == 1 and p > 1:
                        take_block(c, p // (2 * QUADS_PER_BLOCK) - 1)
                take_block(c, BLOCKS - 1)

            act.wait_ge(small_loaded, 48)

            def hidden1(c):
                for m in range(H1 // P):
                    act.wait_ge(l1_done, c * 4 + m + 1)
                    if c >= 2 and m == 0:
                        act.wait_ge(l2_done, (c - 1) * 2)
                    act.activation(h1_sb[:, c % 2, m, :], t_ps[:, m // 2, m % 2, :], ACT.Relu,
                                   bias=b1_sb[:, m:m + 1]).then_inc(h1_made, 1)

            def hidden2(c):
                for m in range(H2 // P):
                    act.wait_ge(l2_done, c * 2 + m + 1)
                    act.activation(h2_sb[:, c, m, :], x_ps[:, m, :], ACT.Relu,
                                   bias=b2_sb[:, m:m + 1]).then_inc(h2_made, 1)

            hidden1(0)
            for c in range(CHUNKS):
                if c + 1 < CHUNKS:
                    hidden1(c + 1)
                hidden2(c)

        @block.vector
        def _(dve):
            dve.memset(selector[:], 0.0).then_inc(selector_zeroed, 1)
            dve.wait_ge(selector_zeroed, 1)
            dve.memset(selector[0:D, 30:31], 1.0).then_inc(constants, 1)
            dve.memset(selector[D:P, 31:32], 1.0).then_inc(constants, 1)
            dve.sem_inc(lo_made, FIELDS - 1)
            dve.sem_inc(products_done, PAIRS)
            for n in range(K_BLOCKS):
                dve.wait_ge(k_rounded, n + 1)
                cols = slice(n * K_BLOCK, (n + 1) * K_BLOCK)
                dve.tensor_tensor(k_split[D:P, cols], k_raw[D:P, n % 2, :], k_split[D:P, cols].bitcast(F32),
                                  op=ALU.subtract).then_inc(k_split_done, 1)

            def take_field(c, f):
                dve.wait_ge(xt_copied, (c + 1) * FIELDS + f + 1)
                dve.tensor_tensor(x_lo[:, f % 2, :], x_ps[:, f % 2, :], x_hi[:, f % 2, :].bitcast(F32),
                                  op=ALU.subtract).then_inc(lo_made, 1)

            def multiply_pair(c, p):
                q = 2 * p
                (j, k), (j2, k2) = GROUPS[q], GROUPS[q + 1]
                if k == 0 or k2 == 0:
                    dve.wait_ge(xt_copied, (c + 1) * FIELDS + (j2 if k2 == 0 else j) + 1)
                dve.wait_ge(t_done, (c + 1) * PAIRS + p + 1)
                dve.wait_ge(summed, (c + 1) * QUADS + p // 2 - 1)
                slot = p % PRODUCT_SLOTS
                if j == j2:
                    last = dve.tensor_tensor(product[:, slot], t_ps[:, p % 2], xt[:, k:k + 2, :], op=ALU.mult)
                else:
                    dve.tensor_tensor(product[:, slot, 0], t_ps[:, p % 2, 0], xt[:, k, :], op=ALU.mult)
                    last = dve.tensor_tensor(product[:, slot, 1], t_ps[:, p % 2, 1], xt[:, k2, :], op=ALU.mult)
                last.then_inc(products_done, 1)

            with dve.Fori(0, CHUNKS) as c:
                for p in range(PAIRS):
                    for f in range(1, FIELDS):
                        if transpose_before_pair(f) == p:
                            take_field(c, f)
                    multiply_pair(c, p)

            dve.wait_ge(l3_done, 1)
            for c in range(CHUNKS):
                dve.tensor_copy(y_sb[32 * c:32 * c + 1, :], z_ps[32 * c:32 * c + 1, 0, :]).then_inc(y_made, 1)


def pair_index(i, j):
    return i * (FIELDS - 1) - i * (i - 1) // 2 + (j - i - 1)


def kernel(**inputs):
    import concourse.bacc as bacc
    from concourse.bass_utils import run_bass_kernel_spmd

    k_in = np.asarray(inputs["L0_rec_kernel"])
    kern = np.zeros((D, NG, 2, D), k_in.dtype)
    w1_in = np.asarray(inputs["W_top1"])
    w1 = np.zeros_like(w1_in)
    for q, (j, k) in enumerate(GROUPS):
        for h in range(2):
            row = z_row(q) + h
            if 2 * k + h < j:
                n = pair_index(2 * k + h, j)
                kern[:, q, h] = k_in[:, n]
                w1[row] = w1_in[n]
            else:
                w1[row] = w1_in[FIELDS * (FIELDS - 1) // 2 + k]

    arrays = {
        "ids": np.ascontiguousarray(inputs["ids"]),
        "dense_t": np.ascontiguousarray(np.asarray(inputs["dense_ctx"]).T),
        "kern": kern.reshape(D, NG * P),
        "w1": w1,
        "b1": np.ascontiguousarray(np.asarray(inputs["b_top1"]).reshape(-1, P).T).reshape(-1),
        "w2": np.ascontiguousarray(inputs["W_top2"]),
        "b2": np.ascontiguousarray(np.asarray(inputs["b_top2"]).reshape(-1, P).T).reshape(-1),
        "w3": np.ascontiguousarray(np.asarray(inputs["W_top3"]).reshape(-1, P).T).reshape(-1),
    }
    for f in range(FIELDS):
        arrays[f"tbl_{f}"] = np.ascontiguousarray(inputs[f"tbl_{f}"])

    nc = bacc.Bacc("TRN2", target_bir_lowering=False, num_devices=1)
    ap = {n: nc.dram_tensor(n, a.shape, mybir.dt.from_np(a.dtype), kind="ExternalInput").ap()
          for n, a in arrays.items()}
    out = nc.dram_tensor("y", (B, 1), F32, kind="ExternalOutput").ap()
    build(nc, ap["ids"], ap["dense_t"], [ap[f"tbl_{f}"] for f in range(FIELDS)], ap["kern"],
          ap["w1"], ap["b1"], ap["w2"], ap["b2"], ap["w3"], out)
    r = run_bass_kernel_spmd(nc, [arrays], core_ids=[0])
    return r.results[0]["y"]
```

```python
import numpy as np
import concourse.bass as bass
import concourse.mybir as mybir
from contextlib import ExitStack

F32 = mybir.dt.float32
F32R = mybir.dt.float32r
I32 = mybir.dt.int32
ALU = mybir.AluOpType
ACT = mybir.ActivationFunctionType

P = 128
B, FIELDS, D = 2048, 32, 64
DENSE = 16
H1, H2 = 512, 256
CHUNK = 512
CHUNKS = B // CHUNK
TILES = CHUNK // P
IDS_HALF = FIELDS // 2

PREFETCHED = 8


def groups_in_order():
    steps = {j: [(j, k) for k in range((j + 1) // 2)] for j in range(1, FIELDS)}
    low = PREFETCHED // 2
    order = [g for j in range(1, FIELDS - 2) for g in steps[j]]
    order += [g for k in range(low) for g in ((FIELDS - 2, k), (FIELDS - 1, k))]
    return order + steps[FIELDS - 2][low:] + steps[FIELDS - 1][low:]


GROUPS = groups_in_order()
NG = len(GROUPS)
QUADS = NG // 4
EARLY = sum((j + 1) // 2 for j in range(1, PREFETCHED)) // 4
LATE = QUADS - EARLY
BLOCKS = 2 * NG // P
QUADS_PER_BLOCK = QUADS // BLOCKS

LATE_QUADS = [(0, q) for q in range(EARLY, QUADS)]
BODY = LATE_QUADS[:-2] + [(1, 0)] + LATE_QUADS[-2:] + [(1, q) for q in range(1, EARLY)]
LAST_BODY = LATE_QUADS
NEXT_FIELDS = {LATE - 7: 0, LATE - 6: 1, LATE - 1: 2, LATE: 3, LATE + 1: 4}
NEXT_LO = {1: (LATE - 6, 0), 2: (LATE - 5, 0), 3: (LATE - 3, 0), 4: (LATE, 0), 5: (LATE, 1),
           6: (LATE + 1, 0), 7: (LATE + 1, 1), 8: (LATE + 2, 0), 9: (LATE + 3, 0)}
PREPARED = len(NEXT_FIELDS)


def first_unit(j):
    return (GROUPS.index((j, 0)) // 4) - EARLY


def last_unit(j):
    return (GROUPS.index((j, (j - 1) // 2)) // 4) - EARLY


FIELD_UNIT = {m: max(first_unit(2 * m) - 3, last_unit(2 * m - 3) + 1 if m > PREPARED else 0)
              for m in range(PREPARED, FIELDS // 2)}

K_COLS = 4 * P
K_AHEAD = 16
LANDING = 4
PRODUCT_SLOTS = 4
LO_BEHIND = 1
X_SLOTS = 4


def x_slot(f):
    return f - 1 if f < 4 else f % X_SLOTS


def x_slot_before(f):
    order = [g for g in range(f - 1, 0, -1)] + [g for g in range(FIELDS - 1, f - 1, -1)]
    return next((g, g >= f) for g in order if x_slot(g) == x_slot(f))


def z_row(q):
    return P * (q // 64) + 32 * (q % 4) + 2 * (q % 64 // 4)


def quads_before(c, q):
    if q >= EARLY:
        body = LAST_BODY if isinstance(c, int) and c == CHUNKS - 1 else BODY
        return c * QUADS + EARLY + body.index((0, q))
    if isinstance(c, int) and c == 0:
        return q
    return (c - 1) * QUADS + EARLY + BODY.index((1, q))


def items_before(c, q, item=0):
    return 2 * quads_before(c, q) + item


def ring_slot(c, q, item, slots):
    return items_before(c if isinstance(c, int) else 1, q, item) % slots


def items_through(c, j, k):
    g = GROUPS.index((j, k))
    return items_before(c, g // 4, g % 4 // 2) + 1


def wait(engine, semaphore, value):
    if not isinstance(value, int) or value > 0:
        engine.wait_ge(semaphore, value)


def run_chunks(engine, first, body, last):
    first()
    body(0)
    with engine.Fori(1, CHUNKS - 1) as c:
        body(c)
    last(CHUNKS - 1)


def build(nc, ids, dense_t, tables, kern, w1, b1, w2, b2, w3, out):
    z_dram = nc.dram_tensor("z_scratch", [CHUNKS, BLOCKS, P, CHUNK], F32, kind="Internal").ap()
    ctx = ExitStack()
    with ctx:
        def sem(name):
            return ctx.enter_context(nc.semaphore(name))

        def sb(name, shape, dt=F32, on=ctx):
            return on.enter_context(nc.sbuf_tensor(name, shape, dt))

        selector = sb("selector", [P, 62])
        identity = sb("identity", [P, P])
        b1_sb = sb("b1_sb", [P, H1 // P])
        b2_sb = sb("b2_sb", [P, H2 // P])
        w3_sb = sb("w3_sb", [P, H2 // P])
        ids_sb = [sb(f"ids_sb{h}", [P, TILES, IDS_HALF], I32) for h in range(2)]

        pair_phase = ExitStack()
        k_split = sb("k_split", [P, NG * P], F32R, pair_phase)
        xt = sb("xt", [P, FIELDS // 2, CHUNK], F32, pair_phase)
        x_hi = sb("x_hi", [P, X_SLOTS, CHUNK], F32R, pair_phase)
        x_lo = sb("x_lo", [P, X_SLOTS, CHUNK], F32R, pair_phase)
        landing = sb("landing", [P, LANDING, TILES, 2, D], F32, pair_phase)
        product = sb("product", [P, PRODUCT_SLOTS, 2, CHUNK], F32, pair_phase)
        k_raw = sb("k_raw", [P, 2, K_COLS], F32, pair_phase)
        z_stage = sb("z_stage", [P, CHUNK], F32, pair_phase)
        pair_phase.close()

        mlp_phase = ExitStack()
        w1_sb = sb("w1_sb", [P, H1 // P, H1], F32, mlp_phase)
        w2_sb = sb("w2_sb", [P, H1 // P, H2], F32, mlp_phase)
        z_sb = sb("z_sb", [P, CHUNKS, BLOCKS, CHUNK], F32, mlp_phase)
        h1_sb = sb("h1_sb", [P, 2, H1 // P, CHUNK], F32, mlp_phase)
        h2_sb = sb("h2_sb", [P, CHUNKS, H2 // P, CHUNK], F32, mlp_phase)
        y_sb = sb("y_sb", [P, CHUNK], F32, mlp_phase)
        mlp_phase.close()
        mlp_bytes = 4 * (4 * H1 + 4 * H2 + CHUNKS * BLOCKS * CHUNK + 2 * 4 * CHUNK + CHUNKS * 2 * CHUNK + CHUNK)
        mlp_quads = -(-mlp_bytes // (4 * K_COLS))

        t_ps = ctx.enter_context(nc.psum_tensor("t_ps", [P, 2, 2, CHUNK], F32))
        x_ps = ctx.enter_context(nc.psum_tensor("x_ps", [P, 2, CHUNK], F32))
        z_ps = ctx.enter_context(nc.psum_tensor("z_ps", [P, 2, CHUNK], F32))

        ids_loaded = [sem(f"ids_loaded{h}") for h in range(2)]
        gathered = [sem(f"gathered{s}") for s in range(LANDING)]
        fields_started = sem("fields_started")
        transposed = sem("transposed")
        xt_copied = sem("xt_copied")
        hi_made = sem("hi_made")
        lo_made = sem("lo_made")
        x_ready = sem("x_ready")
        t_done = sem("t_done")
        products_done = sem("products_done")
        summed = sem("summed")
        z_copied = sem("z_copied")
        z_stored = sem("z_stored")
        k_loaded = [sem(f"k_loaded{s}") for s in range(2)]
        k_rounded = sem("k_rounded")
        k_split_done = sem("k_split_done")
        identity_zeroed = sem("identity_zeroed")
        selector_zeroed = sem("selector_zeroed")
        constants = sem("constants")
        small_loaded = sem("small_loaded")
        w_loaded = sem("w_loaded")
        z_loaded = [sem(f"z_loaded{c}") for c in range(CHUNKS)]
        dense_loaded = [sem(f"dense_loaded{c}") for c in range(CHUNKS)]
        l1_done = sem("l1_done")
        h1_made = sem("h1_made")
        l2_done = sem("l2_done")
        h2_made = sem("h2_made")
        l3_done = sem("l3_done")
        y_made = sem("y_made")
        y_stored = sem("y_stored")

        block = ctx.enter_context(nc.Block())

        @block.sync
        def _(sp):
            def load_ids(c, h):
                rows = ids[bass.ds(c * CHUNK, CHUNK), h * IDS_HALF:(h + 1) * IDS_HALF]
                sp.dma_start(ids_sb[h][:], rows.rearrange("(t p) f -> p t f", p=P)).then_inc(ids_loaded[h], 16)

            def load_k(q):
                wait(sp, k_split_done, q - 1)
                for half in range(2):
                    sp.dma_start(k_raw[half * D:(half + 1) * D, q % 2, :],
                                 kern[:, q * K_COLS:(q + 1) * K_COLS]).then_inc(k_loaded[q % 2], 16)

            def store_block(c, b):
                sp.wait_ge(z_copied, c * BLOCKS + b + 1)
                sp.dma_start(z_dram[bass.ds(c, 1), b].rearrange("a p n -> (a p) n"), z_stage[:])\
                  .then_inc(z_stored, 16)

            def start():
                load_ids(0, 0)
                load_ids(0, 1)
                for q in range(K_AHEAD):
                    load_k(q)
                sp.dma_start(b1_sb[:], b1.rearrange("(p m) -> p m", p=P)).then_inc(small_loaded, 16)
                sp.dma_start(b2_sb[:], b2.rearrange("(p m) -> p m", p=P)).then_inc(small_loaded, 16)
                sp.dma_start(w3_sb[:], w3.rearrange("(p m) -> p m", p=P)).then_inc(small_loaded, 16)

            def body(c):
                for q in range(EARLY, QUADS + 2):
                    if isinstance(c, int) and c == 0 and q - EARLY + K_AHEAD < QUADS:
                        load_k(q - EARLY + K_AHEAD)
                    if (q - 1) % QUADS_PER_BLOCK == 0 and q > QUADS_PER_BLOCK:
                        b = (q - 1) // QUADS_PER_BLOCK - 1
                        store_block(c, b)
                        if b == 0:
                            sp.wait_ge(transposed, c * (FIELDS // 2) + IDS_HALF // 2)
                            load_ids(c + 1, 0)
                        if b == BLOCKS - 1:
                            sp.wait_ge(transposed, (c + 1) * (FIELDS // 2))
                            load_ids(c + 1, 1)

            def last(c):
                for b in range(BLOCKS):
                    store_block(c, b)

            run_chunks(sp, start, body, last)
            sp.wait_ge(y_made, CHUNKS)
            sp.dma_start(out.rearrange("(c n) o -> c (n o)", c=CHUNKS), y_sb[0:97:32, :]).then_inc(y_stored, 16)
            sp.wait_ge(y_stored, 16)

        @block.gpsimd
        def _(pool):
            pool.memset(identity[:], 0.0).then_inc(identity_zeroed, 1)
            pool.wait_ge(identity_zeroed, 1)
            pool.affine_select(out=identity[:], in_=identity[:], compare_op=ALU.not_equal, fill=1.0, base=0,
                               pattern=[[-1, P]], channel_multiplier=1).then_inc(constants, 1)

            def gather_chunk(c):
                for m in range(FIELDS // 2):
                    h = 2 * m // IDS_HALF
                    if 2 * m % IDS_HALF == 0:
                        pool.wait_ge(ids_loaded[h], (c + 1) * 16)
                    wait(pool, transposed, c * (FIELDS // 2) + m - LANDING + 1)
                    pool.sem_inc(fields_started, 1)
                    for a in range(2):
                        col = (2 * m + a) % IDS_HALF
                        for t in range(TILES):
                            pool.indirect_dma_start(
                                out=landing[:, m % LANDING, t, a, :], out_offset=None, in_=tables[2 * m + a][:, :],
                                in_offset=bass.IndirectOffsetOnAxis(ap=ids_sb[h][:, t, col:col + 1], axis=0),
                            ).then_inc(gathered[m % LANDING], 16)

            gather_chunk(0)
            with pool.Fori(1, CHUNKS) as c:
                gather_chunk(c)

            pool.wait_ge(t_done, items_before(CHUNKS - 1, mlp_quads, 1) + 1)
            pool.dma_start(w1_sb[:], w1.rearrange("(k p) n -> p k n", p=P)).then_inc(w_loaded, 16)
            pool.dma_start(w2_sb[:], w2.rearrange("(k p) n -> p k n", p=P)).then_inc(w_loaded, 16)

            def load_z(c):
                pool.wait_ge(z_stored, 16 * BLOCKS * (c + 1))
                pool.dma_start(z_sb[:, c], z_dram[c].rearrange("b p n -> p b n")).then_inc(z_loaded[c], 16)

            def load_dense(c):
                pool.wait_ge(z_loaded[c], 16)
                for m in range(DENSE):
                    row = z_row(GROUPS.index((2 * m + 1, m))) + 1
                    pool.dma_start(z_sb[row % P:row % P + 1, c, row // P, :],
                                   dense_t[m:m + 1, c * CHUNK:(c + 1) * CHUNK]).then_inc(dense_loaded[c], 16)

            for c in range(CHUNKS - 1):
                load_z(c)
            for c in range(CHUNKS - 1):
                load_dense(c)
            load_z(CHUNKS - 1)
            load_dense(CHUNKS - 1)

        @block.tensor
        def _(pe):
            pe.wait_ge(constants, 3)

            def transpose_fields(c, m):
                pe.wait_ge(gathered[m % LANDING], (c * (FIELDS // 2 // LANDING) + m // LANDING + 1) * 16 * 2 * TILES)
                wait(pe, hi_made, c * (FIELDS - 1) + (2 * m - 3 if m >= 2 else 2 * m - 2))
                for t in range(TILES):
                    last = pe.transpose(x_ps[:, m % 2, t * P:(t + 1) * P],
                                        landing[:, m % LANDING, t].rearrange("p a d -> p (a d)"), identity[:])
                last.then_inc(transposed, 1)

            def contract_item(c, q, item):
                before = items_before(c, q, item)
                wait(pe, products_done, before - 1)
                if isinstance(c, int) and c == 0 and item == 0:
                    pe.wait_ge(k_split_done, q + 1)
                slot = ring_slot(c, q, item, 2)
                for g in range(2):
                    n = 4 * q + 2 * item + g
                    j, k = GROUPS[n]
                    if k == 0:
                        pe.wait_ge(x_ready, c * (FIELDS - 1) + j)
                    w = k_split[:, n * P:(n + 1) * P]
                    pe.matmul(t_ps[:, slot, g, :], w, x_hi[:, x_slot(j), :], start=True, stop=False)
                    last = pe.matmul(t_ps[:, slot, g, :], w, x_lo[:, x_slot(j), :], start=False, stop=True)
                last.then_inc(t_done, 1)

            def sum_quad(c, q):
                b, r = q // QUADS_PER_BLOCK, q % QUADS_PER_BLOCK
                if r == 0:
                    wait(pe, z_copied, c * BLOCKS + b - 1)
                pe.wait_ge(products_done, items_before(c, q) + 2)
                for s in range(4):
                    last = pe.matmul(z_ps[32 * s:32 * s + 32, b % 2, :], selector[:, 30 - 2 * r:62 - 2 * r],
                                     product[:, ring_slot(c, q, s // 2, PRODUCT_SLOTS), s % 2, :],
                                     start=(r == 0), stop=(r == QUADS_PER_BLOCK - 1), skip_group_check=True)
                last.then_inc(summed, 1)

            def start():
                transpose_fields(0, 0)
                transpose_fields(0, 1)
                for q in range(EARLY):
                    if q + 2 < PREPARED:
                        transpose_fields(0, q + 2)
                    contract_item(0, q, 0)
                    contract_item(0, q, 1)
                    if q:
                        sum_quad(0, q - 1)

            def body(c, quads=BODY):
                behind = (c, EARLY - 1)
                for u, (dc, q) in enumerate(quads):
                    for m in (m for m in FIELD_UNIT if FIELD_UNIT[m] == u):
                        transpose_fields(c, m)
                    if quads is BODY and u in NEXT_FIELDS:
                        transpose_fields(c + 1, NEXT_FIELDS[u])
                    contract_item(c + dc, q, 0)
                    contract_item(c + dc, q, 1)
                    sum_quad(*behind)
                    behind = (c + dc, q)
                if quads is LAST_BODY:
                    sum_quad(*behind)

            run_chunks(pe, start, body, lambda c: body(c, LAST_BODY))

            pe.wait_ge(w_loaded, 32)
            pe.wait_ge(small_loaded, 48)

            def layer1(c):
                pe.wait_ge(z_loaded[c], 16)
                pe.wait_ge(dense_loaded[c], 16 * DENSE)
                for m in range(H1 // P):
                    if c:
                        pe.wait_ge(h1_made, (c - 1) * 4 + m + 1)
                    for k in range(BLOCKS):
                        last = pe.matmul(t_ps[:, m // 2, m % 2, :], w1_sb[:, k, m * P:(m + 1) * P],
                                         z_sb[:, c, k, :], start=(k == 0), stop=(k == BLOCKS - 1))
                    last.then_inc(l1_done, 1)

            def layer2(c):
                pe.wait_ge(h1_made, (c + 1) * 4)
                for m in range(H2 // P):
                    if c:
                        pe.wait_ge(h2_made, (c - 1) * 2 + m + 1)
                    for k in range(H1 // P):
                        last = pe.matmul(x_ps[:, m, :], w2_sb[:, k, m * P:(m + 1) * P],
                                         h1_sb[:, c % 2, k, :], start=(k == 0), stop=(k == H1 // P - 1))
                    last.then_inc(l2_done, 1)

            layer1(0)
            for c in range(CHUNKS):
                if c + 1 < CHUNKS:
                    layer1(c + 1)
                layer2(c)
            pe.wait_ge(h2_made, CHUNKS * 2)
            pe.wait_ge(z_copied, CHUNKS * BLOCKS)
            for k in range(H2 // P):
                for c in range(CHUNKS):
                    last = pe.matmul(z_ps[32 * c:32 * c + 1, 0, :], w3_sb[:, k:k + 1], h2_sb[:, c, k, :],
                                     start=(k == 0), stop=(k == H2 // P - 1), skip_group_check=True)
            last.then_inc(l3_done, 1)

        @block.scalar
        def _(act):
            def round_k(q):
                act.wait_ge(k_loaded[q % 2], 32 * (q // 2 + 1))
                act.activation(k_split[:, q * K_COLS:(q + 1) * K_COLS], k_raw[:, q % 2, :], ACT.Copy)\
                   .then_inc(k_rounded, 1)

            def take_fields(c, m):
                act.wait_ge(transposed, c * (FIELDS // 2) + m + 1)
                if not (isinstance(c, int) and c == 0):
                    act.wait_ge(products_done, items_through(c - 1, FIELDS - 1, m))
                act.activation(xt[:, m, :], x_ps[:, m % 2, :], ACT.Copy).then_inc(xt_copied, 1)
                fields = [f for f in (2 * m, 2 * m + 1) if f]
                for f in fields:
                    g, earlier = x_slot_before(f)
                    if not earlier:
                        act.wait_ge(t_done, items_through(c, g, (g - 1) // 2))
                    elif not (isinstance(c, int) and c == 0):
                        act.wait_ge(t_done, items_through(c - 1, g, (g - 1) // 2))
                    own = slice(D * (f % 2), D * (f % 2) + D)
                    act.activation(x_hi[0:D, x_slot(f), :], x_ps[own, m % 2, :], ACT.Copy)
                    act.activation(x_hi[D:P, x_slot(f), :], x_ps[own, m % 2, :], ACT.Copy).then_inc(hi_made, 1)
                for f in fields:
                    act.wait_ge(lo_made, c * (FIELDS - 1) + f)
                    own = slice(D * (f % 2), D * (f % 2) + D)
                    other = slice(D - D * (f % 2), P - D * (f % 2))
                    act.activation(x_lo[other, x_slot(f), :], x_lo[own, x_slot(f), :].bitcast(F32), ACT.Copy)\
                       .then_inc(x_ready, 1)

            def take_block(c, b):
                act.wait_ge(summed, quads_before(c, (b + 1) * QUADS_PER_BLOCK - 1) + 1)
                wait(act, z_stored, (c * BLOCKS + b) * 16)
                act.activation(z_stage[:], z_ps[:, b % 2, :], ACT.Copy).then_inc(z_copied, 1)

            def start():
                for q in range(K_AHEAD):
                    round_k(q)
                for m in range(PREPARED):
                    take_fields(0, m)

            def body(c, quads=BODY):
                for u, (dc, q) in enumerate(quads):
                    if isinstance(c, int) and c == 0 and K_AHEAD + u < QUADS:
                        round_k(K_AHEAD + u)
                    for m in (m for m in FIELD_UNIT if FIELD_UNIT[m] == u):
                        take_fields(c, m)
                    if quads is BODY and u in NEXT_FIELDS:
                        take_fields(c + 1, NEXT_FIELDS[u])
                    if u and quads[u - 1][0] == 0 and quads[u - 1][1] % QUADS_PER_BLOCK == QUADS_PER_BLOCK - 1:
                        take_block(c, quads[u - 1][1] // QUADS_PER_BLOCK)
                if quads is LAST_BODY:
                    take_block(c, BLOCKS - 1)

            run_chunks(act, start, body, lambda c: body(c, LAST_BODY))

            act.wait_ge(small_loaded, 48)

            def hidden1(c):
                for m in range(H1 // P):
                    act.wait_ge(l1_done, c * 4 + m + 1)
                    if c >= 2 and m == 0:
                        act.wait_ge(l2_done, (c - 1) * 2)
                    act.activation(h1_sb[:, c % 2, m, :], t_ps[:, m // 2, m % 2, :], ACT.Relu,
                                   bias=b1_sb[:, m:m + 1]).then_inc(h1_made, 1)

            def hidden2(c):
                for m in range(H2 // P):
                    act.wait_ge(l2_done, c * 2 + m + 1)
                    act.activation(h2_sb[:, c, m, :], x_ps[:, m, :], ACT.Relu,
                                   bias=b2_sb[:, m:m + 1]).then_inc(h2_made, 1)

            hidden1(0)
            for c in range(CHUNKS):
                if c + 1 < CHUNKS:
                    hidden1(c + 1)
                hidden2(c)

        @block.vector
        def _(dve):
            dve.memset(selector[:], 0.0).then_inc(selector_zeroed, 1)
            dve.wait_ge(selector_zeroed, 1)
            dve.memset(selector[0:D, 30:31], 1.0).then_inc(constants, 1)
            dve.memset(selector[D:P, 31:32], 1.0).then_inc(constants, 1)

            def split_k(q):
                dve.wait_ge(k_rounded, q + 1)
                cols = slice(q * K_COLS, (q + 1) * K_COLS)
                dve.tensor_tensor(k_split[D:P, cols], k_raw[D:P, q % 2, :], k_split[D:P, cols].bitcast(F32),
                                  op=ALU.subtract).then_inc(k_split_done, 1)

            def take_field(c, f):
                if f:
                    own = slice(D * (f % 2), D * (f % 2) + D)
                    dve.wait_ge(hi_made, c * (FIELDS - 1) + f)
                    dve.tensor_tensor(x_lo[own, x_slot(f), :], xt[own, f // 2, :],
                                      x_hi[own, x_slot(f), :].bitcast(F32), op=ALU.subtract).then_inc(lo_made, 1)

            def multiply_item(c, q, item):
                (j, k), (j2, k2) = GROUPS[4 * q + 2 * item], GROUPS[4 * q + 2 * item + 1]
                if k == 0 or k2 == 0:
                    dve.wait_ge(xt_copied, c * (FIELDS // 2) + max(j, j2) // 2 + 1)
                dve.wait_ge(t_done, items_before(c, q, item) + 1)
                wait(dve, summed, quads_before(c, q) - 1)
                t_slot, slot = ring_slot(c, q, item, 2), ring_slot(c, q, item, PRODUCT_SLOTS)
                if k2 == k + 1:
                    last = dve.tensor_tensor(product[:, slot], t_ps[:, t_slot], xt[:, k:k + 2, :], op=ALU.mult)
                else:
                    dve.tensor_tensor(product[:, slot, 0], t_ps[:, t_slot, 0], xt[:, k, :], op=ALU.mult)
                    last = dve.tensor_tensor(product[:, slot, 1], t_ps[:, t_slot, 1], xt[:, k2, :], op=ALU.mult)
                last.then_inc(products_done, 1)

            def start():
                for q in range(K_AHEAD):
                    split_k(q)
                for f in range(4):
                    take_field(0, f)
                for q in range(EARLY):
                    multiply_item(0, q, 0)
                    multiply_item(0, q, 1)
                    if q + 2 < PREPARED:
                        take_field(0, 2 * q + 4)
                        take_field(0, 2 * q + 5)

            def body(c, quads=BODY):
                for u, (dc, q) in enumerate(quads):
                    for item in range(2):
                        for m in (m for m in FIELD_UNIT if FIELD_UNIT[m] == u - LO_BEHIND):
                            take_field(c, 2 * m + item)
                        if quads is BODY:
                            for f in (f for f in NEXT_LO if NEXT_LO[f] == (u, item)):
                                take_field(c + 1, f)
                        multiply_item(c + dc, q, item)
                    if isinstance(c, int) and c == 0 and K_AHEAD + u < QUADS:
                        split_k(K_AHEAD + u)

            run_chunks(dve, start, body, lambda c: body(c, LAST_BODY))

            dve.wait_ge(l3_done, 1)
            for c in range(CHUNKS):
                dve.tensor_copy(y_sb[32 * c:32 * c + 1, :], z_ps[32 * c:32 * c + 1, 0, :]).then_inc(y_made, 1)


def pair_index(i, j):
    return i * (FIELDS - 1) - i * (i - 1) // 2 + (j - i - 1)


def kernel(**inputs):
    import concourse.bacc as bacc
    from concourse.bass_utils import run_bass_kernel_spmd

    k_in = np.asarray(inputs["L0_rec_kernel"])
    kern = np.zeros((D, NG, 2, D), k_in.dtype)
    w1_in = np.asarray(inputs["W_top1"])
    w1 = np.zeros_like(w1_in)
    for q, (j, k) in enumerate(GROUPS):
        for h in range(2):
            row = z_row(q) + h
            if 2 * k + h < j:
                n = pair_index(2 * k + h, j)
                kern[:, q, h] = k_in[:, n]
                w1[row] = w1_in[n]
            else:
                w1[row] = w1_in[FIELDS * (FIELDS - 1) // 2 + k]

    arrays = {
        "ids": np.ascontiguousarray(inputs["ids"]),
        "dense_t": np.ascontiguousarray(np.asarray(inputs["dense_ctx"]).T),
        "kern": kern.reshape(D, NG * P),
        "w1": w1,
        "b1": np.ascontiguousarray(np.asarray(inputs["b_top1"]).reshape(-1, P).T).reshape(-1),
        "w2": np.ascontiguousarray(inputs["W_top2"]),
        "b2": np.ascontiguousarray(np.asarray(inputs["b_top2"]).reshape(-1, P).T).reshape(-1),
        "w3": np.ascontiguousarray(np.asarray(inputs["W_top3"]).reshape(-1, P).T).reshape(-1),
    }
    for f in range(FIELDS):
        arrays[f"tbl_{f}"] = np.ascontiguousarray(inputs[f"tbl_{f}"])

    nc = bacc.Bacc("TRN2", target_bir_lowering=False, num_devices=1)
    ap = {n: nc.dram_tensor(n, a.shape, mybir.dt.from_np(a.dtype), kind="ExternalInput").ap()
          for n, a in arrays.items()}
    out = nc.dram_tensor("y", (B, 1), F32, kind="ExternalOutput").ap()
    build(nc, ap["ids"], ap["dense_t"], [ap[f"tbl_{f}"] for f in range(FIELDS)], ap["kern"],
          ap["w1"], ap["b1"], ap["w2"], ap["b2"], ap["w3"], out)
    r = run_bass_kernel_spmd(nc, [arrays], core_ids=[0])
    return r.results[0]["y"]
```

```python
import numpy as np
import concourse.bass as bass
import concourse.mybir as mybir
from contextlib import ExitStack

F32 = mybir.dt.float32
F32R = mybir.dt.float32r
I32 = mybir.dt.int32
ALU = mybir.AluOpType
ACT = mybir.ActivationFunctionType

P = 128
B, FIELDS, D = 2048, 32, 64
DENSE = 16
H1, H2 = 512, 256
CHUNK = 512
CHUNKS = B // CHUNK
TILES = CHUNK // P
IDS_HALF = FIELDS // 2

PREFETCHED = 8


def groups_in_order():
    steps = {j: [(j, k) for k in range((j + 1) // 2)] for j in range(1, FIELDS)}
    low = PREFETCHED // 2
    order = [g for j in range(1, FIELDS - 2) for g in steps[j]]
    order += [g for k in range(low) for g in ((FIELDS - 2, k), (FIELDS - 1, k))]
    return order + steps[FIELDS - 2][low:] + steps[FIELDS - 1][low:]


GROUPS = groups_in_order()
NG = len(GROUPS)
K_WIDTH = (FIELDS * (FIELDS - 1) // 2 + 1) * D
QUADS = NG // 4
EARLY = sum((j + 1) // 2 for j in range(1, PREFETCHED)) // 4
LATE = QUADS - EARLY
BLOCKS = 2 * NG // P
QUADS_PER_BLOCK = QUADS // BLOCKS

LATE_QUADS = [(0, q) for q in range(EARLY, QUADS)]
BODY = LATE_QUADS[:-3] + [(1, 0)] + LATE_QUADS[-3:] + [(1, q) for q in range(1, EARLY)]
LAST_BODY = LATE_QUADS
NEXT_FIELDS = {LATE - 8: 0, LATE - 5: 1, LATE - 3: 2, LATE: 3, LATE + 2: 4}
PIECE_UNITS = (45, 48, 52, 55, 58)
PREPARED = len(NEXT_FIELDS)


def k_col(n):
    return D * sum(2 if 2 * k + 1 < j else 1 for j, k in GROUPS[:n])


def first_unit(j):
    return (GROUPS.index((j, 0)) // 4) - EARLY


def last_unit(j):
    return (GROUPS.index((j, (j - 1) // 2)) // 4) - EARLY


FIELD_LEAD = 3
FIELD_UNIT = {m: max(first_unit(2 * m) - FIELD_LEAD, last_unit(2 * m - 3) + 1 if m > PREPARED else 0)
              for m in range(PREPARED, FIELDS // 2)}

K_PARTS = 32
K_COLS = K_WIDTH // K_PARTS
assert K_COLS * K_PARTS == K_WIDTH
K_LOADS = K_PARTS // 2
K_SLOTS = 4
HI_AFTER_K = {8: 0, 13: 1, 18: 2, 22: 3, 27: 4}
LO_AFTER_K = {6: 0, 11: 1, 15: 2, 19: 3, 23: 4}
PRODUCTS_AFTER_K = {12: 0, 17: 1, 21: 2, 23: 3}
K_PARTS_FIRST = 28
LANDING = 4
T_SLOTS = 3
PRODUCT_SLOTS = 5
LO_BEHIND = 1
X_SLOTS = 5
X_ROUNDS = (4, 5, 5, 4, 4, 4, 5)
X_ORDER = [s for n in X_ROUNDS for s in range(n)]
assert len(X_ORDER) == FIELDS - 1 and max(X_ROUNDS) == X_SLOTS


def x_slot(f):
    return X_ORDER[f - 1]


def x_slot_before(f):
    order = [g for g in range(f - 1, 0, -1)] + [g for g in range(FIELDS - 1, f - 1, -1)]
    return next((g, g >= f) for g in order if x_slot(g) == x_slot(f))


EARLY_ROWS = 2 * EARLY
Z_LOADS = 1 + 2 * 4


def z_place(q):
    return ((q - EARLY) // QUADS_PER_BLOCK, (q - EARLY) % QUADS_PER_BLOCK) if q >= EARLY \
        else (BLOCKS - 1, QUADS_PER_BLOCK - EARLY + q)


def z_row(n):
    b, r = z_place(n // 4)
    return P * b + 32 * (n % 4) + 2 * r


def quads_before(c, q):
    if q >= EARLY:
        body = LAST_BODY if isinstance(c, int) and c == CHUNKS - 1 else BODY
        return c * QUADS + EARLY + body.index((0, q))
    if isinstance(c, int) and c == 0:
        return q
    return (c - 1) * QUADS + EARLY + BODY.index((1, q))


def items_before(c, q, item=0):
    return 2 * quads_before(c, q) + item


def place(c, q, item=0):
    if q >= EARLY:
        return 2 * (LAST_BODY if isinstance(c, int) and c == CHUNKS - 1 else BODY).index((0, q)) + item
    return 2 * (q if isinstance(c, int) and c == 0 else BODY.index((1, q))) + item


def t_slot(c, q, item):
    return place(c, q, item) % T_SLOTS


def t_slot_free(c, q, item):
    n, length = place(c, q, item), 2 * len(BODY)
    before = [x for x in range(n - 1, -1, -1) if x % T_SLOTS == n % T_SLOTS]
    if before:
        return items_before(c, q, item) - n + before[0] + 1
    assert 2 * EARLY % T_SLOTS == length % T_SLOTS
    last = next(x for x in range(length - 1, -1, -1) if x % T_SLOTS == n % T_SLOTS)
    return items_before(c, q, item) - n - (length - last) + 1


SHORT_ROUNDS = -2 * len(BODY) % PRODUCT_SLOTS
PRODUCT_ORDER = [s for n in range(2 * len(BODY)) for s in range(PRODUCT_SLOTS - (n % 8 == 4 and n // 8 < SHORT_ROUNDS))]\
    [:2 * len(BODY)]
assert PRODUCT_ORDER[-1] == PRODUCT_SLOTS - 1


def product_slot(c, q, item):
    return PRODUCT_ORDER[place(c, q, item)]


def product_slot_free(c, q, item):
    n = place(c, q, item)
    quads = quads_before(c, q)
    if isinstance(c, int) and c == 0 and q < EARLY:
        before = [x for x in range(n) if PRODUCT_ORDER[x] == PRODUCT_ORDER[n]]
        return before[-1] // 2 + 1 if before else 0
    before = [x for x in range(n) if PRODUCT_ORDER[x] == PRODUCT_ORDER[n]]
    if before:
        return quads - n // 2 + before[-1] // 2 + 1
    if isinstance(c, int) and c == 0:
        before = [x for x in range(2 * EARLY) if PRODUCT_ORDER[x] == PRODUCT_ORDER[n]]
        return before[-1] // 2 + 1
    before = [x for x in range(2 * len(BODY)) if PRODUCT_ORDER[x] == PRODUCT_ORDER[n]]
    return quads - n // 2 - len(BODY) + before[-1] // 2 + 1


def items_through(c, j, k):
    g = GROUPS.index((j, k))
    return items_before(c, g // 4, g % 4 // 2) + 1


def wait(engine, semaphore, value):
    if not isinstance(value, int) or value > 0:
        engine.wait_ge(semaphore, value)


def run_chunks(engine, first, body, last):
    first()
    body(0)
    with engine.Fori(1, CHUNKS - 1) as c:
        body(c)
    last(CHUNKS - 1)


def build(nc, ids, dense_t, tables, kern, w1, b1, w2, b2, w3, out):
    z_dram = nc.dram_tensor("z_scratch", [CHUNKS + 1, BLOCKS, P, CHUNK], F32, kind="Internal").ap()
    ctx = ExitStack()
    with ctx:
        def sem(name):
            return ctx.enter_context(nc.semaphore(name))

        def sb(name, shape, dt=F32, on=ctx):
            return on.enter_context(nc.sbuf_tensor(name, shape, dt))

        selector = sb("selector", [P, 62])
        identity = sb("identity", [P, P])
        b1_sb = sb("b1_sb", [P, H1 // P])
        b2_sb = sb("b2_sb", [P, H2 // P])
        w3_sb = sb("w3_sb", [P, H2 // P])
        ids_sb = [sb(f"ids_sb{h}", [P, TILES, IDS_HALF], I32) for h in range(2)]

        pair_phase = ExitStack()
        k_split = sb("k_split", [P, K_WIDTH], F32R, pair_phase)
        xt = sb("xt", [P, FIELDS // 2, CHUNK], F32, pair_phase)
        x_hi = sb("x_hi", [P, X_SLOTS, CHUNK], F32R, pair_phase)
        x_lo = sb("x_lo", [P, X_SLOTS, CHUNK], F32R, pair_phase)
        landing = sb("landing", [P, LANDING, TILES, 2, D], F32, pair_phase)
        product = sb("product", [P, PRODUCT_SLOTS, 2, CHUNK], F32, pair_phase)
        k_raw = xt[:, FIELDS // 2 - 2 * K_SLOTS:, :].rearrange("p (s a) n -> p s (a n)", s=K_SLOTS)[:, :, 0:K_COLS]
        z_stage = sb("z_stage", [P, CHUNK], F32, pair_phase)
        pair_phase.close()

        mlp_phase = ExitStack()
        w1_hi = sb("w1_hi", [P, H1 // P, H1], F32R, mlp_phase)
        w2_hi = sb("w2_hi", [P, H1 // P, H2], F32R, mlp_phase)
        z_hi = sb("z_hi", [P, 2, BLOCKS, CHUNK], F32R, mlp_phase)

        def operands(part, dt, on):
            return (sb(f"w1_{part}", [P, H1 // P, H1], dt, on), sb(f"w2_{part}", [P, H1 // P, H2], dt, on),
                    sb(f"z_{part}", [P, CHUNKS, BLOCKS, CHUNK], dt, on), sb(f"h1_{part}", [P, 2, H1 // P, CHUNK], dt, on))

        raw_phase = ExitStack()
        w1_raw, w2_raw, z_raw, h1_raw = operands("raw", F32, raw_phase)
        raw_phase.close()
        w1_lo, w2_lo, z_lo, h1_lo = operands("lo", F32R, mlp_phase)
        h1_hi = sb("h1_hi", [P, 2, H1 // P, CHUNK], F32R, mlp_phase)
        h2_sb = sb("h2_sb", [P, CHUNKS, H2 // P, CHUNK], F32, mlp_phase)
        y_sb = sb("y_sb", [P, CHUNK], F32, mlp_phase)
        mlp_phase.close()
        early_columns = 2 * (4 * H1 + 4 * H2) + (CHUNKS + 2) * BLOCKS * CHUNK
        mlp_group = max(n for n in range(NG) if k_col(n) < early_columns)

        t_ps = ctx.enter_context(nc.psum_tensor("t_ps", [P, T_SLOTS, 2, CHUNK], F32))
        x_ps = ctx.enter_context(nc.psum_tensor("x_ps", [P, CHUNK], F32))
        z_ps = ctx.enter_context(nc.psum_tensor("z_ps", [P, CHUNK], F32))

        ids_loaded = [sem(f"ids_loaded{h}") for h in range(2)]
        gathered = [sem(f"gathered{s}") for s in range(LANDING)]
        fields_started = sem("fields_started")
        transposed = sem("transposed")
        xt_copied = sem("xt_copied")
        hi_made = sem("hi_made")
        lo_made = sem("lo_made")
        x_ready = sem("x_ready")
        t_done = sem("t_done")
        products_done = sem("products_done")
        summed = sem("summed")
        z_copied = sem("z_copied")
        z_stored = sem("z_stored")
        dense_stored = sem("dense_stored")
        k_loaded = [sem(f"k_loaded{s}") for s in range(K_SLOTS)]
        k_rounded = sem("k_rounded")
        k_split_done = sem("k_split_done")
        identity_zeroed = sem("identity_zeroed")
        selector_zeroed = sem("selector_zeroed")
        constants = sem("constants")
        small_loaded = sem("small_loaded")
        w_loaded = sem("w_loaded")
        z_loaded = [sem(f"z_loaded{c}") for c in range(CHUNKS)]
        mlp_hi_made = sem("mlp_hi_made")
        mlp_lo_made = sem("mlp_lo_made")
        l1_done = sem("l1_done")
        h1_made = sem("h1_made")
        h1_hi_made = sem("h1_hi_made")
        h1_lo_made = sem("h1_lo_made")
        l2_done = sem("l2_done")
        h2_made = sem("h2_made")
        l3_done = sem("l3_done")
        y_made = sem("y_made")
        y_stored = sem("y_stored")

        mlp_pieces = [tuple(t[:, rows, :] for t in (w1_raw, w1_hi, w1_lo)) for rows in (slice(0, 2), slice(2, 4))]
        mlp_pieces += [(w2_raw[:], w2_hi[:], w2_lo[:])]
        mlp_pieces += [tuple(t[:, 0, blocks, :] for t in (z_raw, z_hi, z_lo)) for blocks in (slice(0, 2), slice(2, 4))]
        mlp_pieces += [(z_raw[:, c], z_hi[:, c % 2], z_lo[:, c]) for c in range(1, CHUNKS)]
        assert len(mlp_pieces) == len(PIECE_UNITS) + CHUNKS - 1

        block = ctx.enter_context(nc.Block())

        @block.sync
        def _(sp):
            def load_ids(c, h):
                rows = ids[bass.ds(c * CHUNK, CHUNK), h * IDS_HALF:(h + 1) * IDS_HALF]
                sp.dma_start(ids_sb[h][:], rows.rearrange("(t p) f -> p t f", p=P)).then_inc(ids_loaded[h], 16)

            def load_k(n):
                wait(sp, k_split_done, 2 * (n - K_SLOTS + 1))
                sp.dma_start(k_raw[:, n % K_SLOTS, :], kern[n]).then_inc(k_loaded[n % K_SLOTS], 16)

            def store_block(c, b):
                sp.wait_ge(z_copied, c * BLOCKS + b + 2)
                sp.dma_start(z_dram[bass.ds(c + 1, 1), b].rearrange("a p n -> (a p) n"), z_stage[:])\
                  .then_inc(z_stored, 16)

            def insert_dense(body_c, c, b, early):
                for m in range(DENSE):
                    n = GROUPS.index((2 * m + 1, m))
                    row = z_row(n) + 1
                    if row // P == b and (n // 4 < EARLY) == early:
                        sp.dma_start(z_dram[bass.ds(body_c + 1, 1), b, row % P, :],
                                     dense_t[m:m + 1, bass.ds(c * CHUNK, CHUNK)]).then_inc(dense_stored, 16)

            def finish_block(c, b, next_chunk=True):
                store_block(c, b)
                sp.wait_ge(z_stored, (c * BLOCKS + b + 2) * 16)
                insert_dense(c, c, b, False)
                if b == BLOCKS - 1 and next_chunk:
                    insert_dense(c, c + 1, b, True)

            def load_z(c):
                sp.wait_ge(dense_stored, 16 * (DENSE * (c + 1) + (PREFETCHED // 2 if c < CHUNKS - 1 else 0)))
                sp.dma_start(z_raw[:, c, 0:BLOCKS - 1], z_dram[c + 1, 0:BLOCKS - 1].rearrange("b p n -> p b n"))\
                  .then_inc(z_loaded[c], 16)
                own_rows = 32 - EARLY_ROWS
                for s in range(4):
                    for body, lo, hi in ((c + 1, 32 * s, 32 * s + own_rows), (c, 32 * s + own_rows, 32 * s + 32)):
                        sp.dma_start(z_raw[lo:hi, c, BLOCKS - 1], z_dram[body, BLOCKS - 1, lo:hi])\
                          .then_inc(z_loaded[c], 16)

            def start():
                load_ids(0, 0)
                load_ids(0, 1)
                for n in range(K_LOADS):
                    load_k(n)
                sp.dma_start(b1_sb[:], b1.rearrange("(p m) -> p m", p=P)).then_inc(small_loaded, 16)
                sp.dma_start(b2_sb[:], b2.rearrange("(p m) -> p m", p=P)).then_inc(small_loaded, 16)
                sp.dma_start(w3_sb[:], w3.rearrange("(p m) -> p m", p=P)).then_inc(small_loaded, 16)
                store_block(-1, BLOCKS - 1)
                sp.wait_ge(z_stored, 16)
                insert_dense(-1, 0, BLOCKS - 1, True)

            def body(c):
                for b in range(BLOCKS):
                    finish_block(c, b)
                    if b == 0:
                        sp.wait_ge(transposed, c * (FIELDS // 2) + IDS_HALF // 2)
                        load_ids(c + 1, 0)
                    if b == BLOCKS - 2:
                        sp.wait_ge(transposed, (c + 1) * (FIELDS // 2))
                        load_ids(c + 1, 1)

            def last(c):
                for b in range(BLOCKS):
                    finish_block(c, b, next_chunk=False)
                    if b == 1:
                        sp.wait_ge(t_done, items_through(c, *GROUPS[mlp_group]))
                        sp.dma_start(w1_raw[:], w1.rearrange("(k p) n -> p k n", p=P)).then_inc(w_loaded, 16)
                        sp.dma_start(w2_raw[:], w2.rearrange("(k p) n -> p k n", p=P)).then_inc(w_loaded, 16)
                        for earlier in range(c):
                            load_z(earlier)
                load_z(c)

            run_chunks(sp, start, body, last)
            sp.wait_ge(y_made, CHUNKS)
            sp.dma_start(out.rearrange("(c n) o -> c (n o)", c=CHUNKS), y_sb[0:97:32, :]).then_inc(y_stored, 16)
            sp.wait_ge(y_stored, 16)

        @block.gpsimd
        def _(pool):
            pool.memset(identity[:], 0.0).then_inc(identity_zeroed, 1)
            pool.wait_ge(identity_zeroed, 1)
            pool.affine_select(out=identity[:], in_=identity[:], compare_op=ALU.not_equal, fill=1.0, base=0,
                               pattern=[[-1, P]], channel_multiplier=1).then_inc(constants, 1)

            def gather_chunk(c):
                for m in range(FIELDS // 2):
                    h = 2 * m // IDS_HALF
                    if 2 * m % IDS_HALF == 0:
                        pool.wait_ge(ids_loaded[h], (c + 1) * 16)
                    wait(pool, transposed, c * (FIELDS // 2) + m - LANDING + 1)
                    pool.sem_inc(fields_started, 1)
                    for a in range(2):
                        col = (2 * m + a) % IDS_HALF
                        for t in range(TILES):
                            pool.indirect_dma_start(
                                out=landing[:, m % LANDING, t, a, :], out_offset=None, in_=tables[2 * m + a][:, :],
                                in_offset=bass.IndirectOffsetOnAxis(ap=ids_sb[h][:, t, col:col + 1], axis=0),
                            ).then_inc(gathered[m % LANDING], 16)

            gather_chunk(0)
            with pool.Fori(1, CHUNKS) as c:
                gather_chunk(c)

        @block.tensor
        def _(pe):
            pe.wait_ge(constants, 3)

            def transpose_fields(c, m):
                pe.wait_ge(gathered[m % LANDING], (c * (FIELDS // 2 // LANDING) + m // LANDING + 1) * 16 * 2 * TILES)
                wait(pe, hi_made, c * (FIELDS - 1) + max(2 * m - 1, 0))
                for t in range(TILES):
                    last = pe.transpose(x_ps[:, t * P:(t + 1) * P],
                                        landing[:, m % LANDING, t].rearrange("p a d -> p (a d)"), identity[:])
                last.then_inc(transposed, 1)

            def contract_item(c, q, item):
                wait(pe, products_done, t_slot_free(c, q, item))
                if isinstance(c, int) and c == 0 and item == 0:
                    pe.wait_ge(k_split_done, -(-(k_col(4 * q + 3) + P) // K_COLS))
                slot = t_slot(c, q, item)
                for g in range(2):
                    n = 4 * q + 2 * item + g
                    j, k = GROUPS[n]
                    if k == 0:
                        pe.wait_ge(x_ready, c * (FIELDS - 1) + j)
                    w = k_split[:, k_col(n):k_col(n) + P]
                    pe.matmul(t_ps[:, slot, g, :], w, x_hi[:, x_slot(j), :], start=True, stop=False)
                    last = pe.matmul(t_ps[:, slot, g, :], w, x_lo[:, x_slot(j), :], start=False, stop=True)
                last.then_inc(t_done, 1)

            def sum_quad(c, q, first, last_one, block_before):
                if first:
                    wait(pe, z_copied, block_before)
                r = z_place(q)[1]
                pe.wait_ge(products_done, items_before(c, q) + 2)
                for s in range(4):
                    last = pe.matmul(z_ps[32 * s:32 * s + 32, :], selector[:, 30 - 2 * r:62 - 2 * r],
                                     product[:, product_slot(c, q, s // 2), s % 2, :],
                                     start=first, stop=last_one, skip_group_check=True)
                last.then_inc(summed, 1)

            def start():
                transpose_fields(0, 0)
                transpose_fields(0, 1)
                for q in range(EARLY):
                    contract_item(0, q, 0)
                    contract_item(0, q, 1)
                    if q + 2 < PREPARED:
                        transpose_fields(0, q + 2)
                    if q % 2 == 0 and q:
                        sum_quad(0, q - 2, q == 2, False, 0)
                        sum_quad(0, q - 1, False, False, 0)

            def body(c, quads=BODY):
                def sum_unit(u):
                    if u < 0:
                        return sum_quad(c, EARLY + u, False, u == -1, 0)
                    dc, q = quads[u]
                    b, r = u // QUADS_PER_BLOCK, u % QUADS_PER_BLOCK
                    sum_quad(c + dc, q, r == 0, r == QUADS_PER_BLOCK - 1 or u == len(quads) - 1, c * BLOCKS + b + 1)

                for u, (dc, q) in enumerate(quads):
                    for m in (m for m in FIELD_UNIT if FIELD_UNIT[m] == u):
                        transpose_fields(c, m)
                    if quads is BODY and u in NEXT_FIELDS:
                        transpose_fields(c + 1, NEXT_FIELDS[u])
                    contract_item(c + dc, q, 0)
                    contract_item(c + dc, q, 1)
                    if u % 2 == 0:
                        sum_unit(u - 2)
                        sum_unit(u - 1)
                if quads is LAST_BODY:
                    sum_unit(len(quads) - 2)
                    sum_unit(len(quads) - 1)

            run_chunks(pe, start, body, lambda c: body(c, LAST_BODY))

            pe.wait_ge(small_loaded, 48)

            def layer1(c):
                pe.wait_ge(mlp_lo_made, len(PIECE_UNITS) + c)
                for m in range(H1 // P):
                    if c:
                        pe.wait_ge(h1_made, (c - 1) * 4 + m + 1)
                    out_cols = slice(m * P, (m + 1) * P)
                    for k in range(BLOCKS):
                        bank = t_ps[:, m // 2, m % 2, :]
                        pe.matmul(bank, w1_hi[:, k, out_cols], z_hi[:, c % 2, k, :], start=(k == 0), stop=False)
                        pe.matmul(bank, w1_hi[:, k, out_cols], z_lo[:, c, k, :], start=False, stop=False)
                        last = pe.matmul(bank, w1_lo[:, k, out_cols], z_hi[:, c % 2, k, :],
                                         start=False, stop=(k == BLOCKS - 1))
                    last.then_inc(l1_done, 1)

            def layer2(c):
                pe.wait_ge(h1_lo_made, (c + 1) * 4)
                for m in range(H2 // P):
                    if c:
                        pe.wait_ge(h2_made, (c - 1) * 2 + m + 1)
                    out_cols = slice(m * P, (m + 1) * P)
                    for k in range(H1 // P):
                        bank = t_ps[:, 2, m, :]
                        pe.matmul(bank, w2_hi[:, k, out_cols], h1_hi[:, c % 2, k, :], start=(k == 0), stop=False)
                        pe.matmul(bank, w2_hi[:, k, out_cols], h1_lo[:, c % 2, k, :], start=False, stop=False)
                        last = pe.matmul(bank, w2_lo[:, k, out_cols], h1_hi[:, c % 2, k, :],
                                         start=False, stop=(k == H1 // P - 1))
                    last.then_inc(l2_done, 1)

            layer1(0)
            for c in range(CHUNKS):
                if c + 1 < CHUNKS:
                    layer1(c + 1)
                layer2(c)
            pe.wait_ge(h2_made, CHUNKS * 2)
            pe.wait_ge(z_copied, CHUNKS * BLOCKS + 1)
            for k in range(H2 // P):
                for c in range(CHUNKS):
                    last = pe.matmul(z_ps[32 * c:32 * c + 1, :], w3_sb[:, k:k + 1], h2_sb[:, c, k, :],
                                     start=(k == 0), stop=(k == H2 // P - 1), skip_group_check=True)
            last.then_inc(l3_done, 1)

        @block.scalar
        def _(act):
            def round_k(n):
                load, raw = n // 2, slice(D * (n % 2), D * (n % 2) + D)
                if n % 2 == 0:
                    act.wait_ge(k_loaded[load % K_SLOTS], 16 * (load // K_SLOTS + 1))
                act.activation(k_split[raw, n * K_COLS:(n + 1) * K_COLS], k_raw[raw, load % K_SLOTS, :], ACT.Copy)\
                   .then_inc(k_rounded, 1)

            def take_fields(c, m):
                act.wait_ge(transposed, c * (FIELDS // 2) + m + 1)
                if not (isinstance(c, int) and c == 0):
                    act.wait_ge(products_done, items_through(c - 1, FIELDS - 1, m))
                elif m == FIELDS // 2 - 2 * K_SLOTS:
                    act.wait_ge(k_split_done, K_PARTS)
                act.activation(xt[:, m, :], x_ps[:], ACT.Copy).then_inc(xt_copied, 1)
                fields = [f for f in (2 * m, 2 * m + 1) if f]
                for f in fields:
                    g, earlier = x_slot_before(f)
                    if not earlier:
                        act.wait_ge(t_done, items_through(c, g, (g - 1) // 2))
                    elif not (isinstance(c, int) and c == 0):
                        act.wait_ge(t_done, items_through(c - 1, g, (g - 1) // 2))
                    own = slice(D * (f % 2), D * (f % 2) + D)
                    act.activation(x_hi[0:D, x_slot(f), :], x_ps[own, :], ACT.Copy)
                    act.activation(x_hi[D:P, x_slot(f), :], x_ps[own, :], ACT.Copy).then_inc(hi_made, 1)
                for f in fields:
                    act.wait_ge(lo_made, c * (FIELDS - 1) + f)
                    own = slice(D * (f % 2), D * (f % 2) + D)
                    other = slice(D - D * (f % 2), P - D * (f % 2))
                    act.activation(x_lo[other, x_slot(f), :], x_lo[own, x_slot(f), :].bitcast(F32), ACT.Copy)\
                       .then_inc(x_ready, 1)

            def take_block(n, quads):
                act.wait_ge(summed, quads)
                wait(act, z_stored, n * 16)
                act.activation(z_stage[:], z_ps[:], ACT.Copy).then_inc(z_copied, 1)

            def round_piece(n):
                if n == 0:
                    act.wait_ge(w_loaded, 32)
                c = max(n - len(PIECE_UNITS) + 1, 0)
                if n == len(PIECE_UNITS) - 2 or c:
                    act.wait_ge(z_loaded[c], 16 * Z_LOADS)
                if c >= 2:
                    act.wait_ge(l1_done, (c - 1) * 4)
                raw, hi, _ = mlp_pieces[n]
                act.activation(hi, raw, ACT.Copy).then_inc(mlp_hi_made, 1)

            def start():
                for n in range(K_PARTS):
                    round_k(n)
                    if n in HI_AFTER_K:
                        take_fields(0, HI_AFTER_K[n])

            def body(c, quads=BODY):
                for u in range(len(quads)):
                    for m in (m for m in FIELD_UNIT if FIELD_UNIT[m] == u):
                        take_fields(c, m)
                    if quads is BODY and u in NEXT_FIELDS:
                        take_fields(c + 1, NEXT_FIELDS[u])
                    if quads is LAST_BODY and u in PIECE_UNITS:
                        round_piece(PIECE_UNITS.index(u))
                    if u % QUADS_PER_BLOCK == 0:
                        take_block(c * BLOCKS + u // QUADS_PER_BLOCK, c * QUADS + EARLY + u)
                if quads is LAST_BODY:
                    take_block((c + 1) * BLOCKS, c * QUADS + EARLY + len(quads))

            run_chunks(act, start, body, lambda c: body(c, LAST_BODY))

            act.wait_ge(small_loaded, 48)

            def hidden1(c):
                for m in range(H1 // P):
                    act.wait_ge(l1_done, c * 4 + m + 1)
                    if c >= 2 and m == 0:
                        act.wait_ge(l2_done, (c - 1) * 2)
                    raw = h1_raw[:, c % 2, m, :]
                    act.activation(raw, t_ps[:, m // 2, m % 2, :], ACT.Relu, bias=b1_sb[:, m:m + 1]).then_inc(h1_made, 1)
                    act.wait_ge(h1_made, c * 4 + m + 1)
                    act.activation(h1_hi[:, c % 2, m, :], raw, ACT.Copy).then_inc(h1_hi_made, 1)

            def hidden2(c):
                for m in range(H2 // P):
                    act.wait_ge(l2_done, c * 2 + m + 1)
                    act.activation(h2_sb[:, c, m, :], t_ps[:, 2, m, :], ACT.Relu,
                                   bias=b2_sb[:, m:m + 1]).then_inc(h2_made, 1)

            round_piece(len(PIECE_UNITS))
            hidden1(0)
            for c in range(CHUNKS):
                if c + 2 < CHUNKS:
                    round_piece(len(PIECE_UNITS) + c + 1)
                if c + 1 < CHUNKS:
                    hidden1(c + 1)
                hidden2(c)

        @block.vector
        def _(dve):
            dve.memset(selector[:], 0.0).then_inc(selector_zeroed, 1)
            dve.wait_ge(selector_zeroed, 1)
            dve.memset(selector[0:D, 30:31], 1.0).then_inc(constants, 1)
            dve.memset(selector[D:P, 31:32], 1.0).then_inc(constants, 1)

            def split_k(n):
                dve.wait_ge(k_rounded, n + 1)
                cols, raw = slice(n * K_COLS, (n + 1) * K_COLS), slice(D * (n % 2), D * (n % 2) + D)
                other = slice(D - D * (n % 2), P - D * (n % 2))
                dve.tensor_tensor(k_split[other, cols], k_raw[raw, n // 2 % K_SLOTS, :],
                                  k_split[raw, cols].bitcast(F32), op=ALU.subtract).then_inc(k_split_done, 1)

            def take_field(c, f):
                if f:
                    own = slice(D * (f % 2), D * (f % 2) + D)
                    dve.wait_ge(hi_made, c * (FIELDS - 1) + f)
                    dve.tensor_tensor(x_lo[own, x_slot(f), :], xt[own, f // 2, :],
                                      x_hi[own, x_slot(f), :].bitcast(F32), op=ALU.subtract).then_inc(lo_made, 1)

            def split_piece(n):
                dve.wait_ge(mlp_hi_made, n + 1)
                raw, hi, lo = mlp_pieces[n]
                dve.tensor_tensor(lo, raw, hi.bitcast(F32), op=ALU.subtract).then_inc(mlp_lo_made, 1)

            def multiply_item(c, q, item):
                (j, k), (j2, k2) = GROUPS[4 * q + 2 * item], GROUPS[4 * q + 2 * item + 1]
                if k == 0 or k2 == 0:
                    dve.wait_ge(xt_copied, c * (FIELDS // 2) + max(j, j2) // 2 + 1)
                dve.wait_ge(t_done, items_before(c, q, item) + 1)
                wait(dve, summed, product_slot_free(c, q, item))
                t, slot = t_slot(c, q, item), product_slot(c, q, item)
                if k2 == k + 1:
                    last = dve.tensor_tensor(product[:, slot], t_ps[:, t], xt[:, k:k + 2, :], op=ALU.mult)
                else:
                    dve.tensor_tensor(product[:, slot, 0], t_ps[:, t, 0], xt[:, k, :], op=ALU.mult)
                    last = dve.tensor_tensor(product[:, slot, 1], t_ps[:, t, 1], xt[:, k2, :], op=ALU.mult)
                last.then_inc(products_done, 1)

            def start():
                for n in range(K_PARTS_FIRST):
                    split_k(n)
                    if n in LO_AFTER_K:
                        take_field(0, 2 * LO_AFTER_K[n])
                        take_field(0, 2 * LO_AFTER_K[n] + 1)
                    if n in PRODUCTS_AFTER_K:
                        multiply_item(0, PRODUCTS_AFTER_K[n], 0)
                        multiply_item(0, PRODUCTS_AFTER_K[n], 1)

            def body(c, quads=BODY):
                for u, (dc, q) in enumerate(quads):
                    if quads is LAST_BODY and u - LO_BEHIND in PIECE_UNITS:
                        split_piece(PIECE_UNITS.index(u - LO_BEHIND))
                    if isinstance(c, int) and c == 0 and K_PARTS_FIRST + u < K_PARTS:
                        split_k(K_PARTS_FIRST + u)
                    for item in range(2):
                        for m in (m for m in FIELD_UNIT if FIELD_UNIT[m] == u - LO_BEHIND):
                            take_field(c, 2 * m + item)
                        if quads is BODY and u - LO_BEHIND in NEXT_FIELDS:
                            take_field(c + 1, 2 * NEXT_FIELDS[u - LO_BEHIND] + item)
                        multiply_item(c + dc, q, item)

            run_chunks(dve, start, body, lambda c: body(c, LAST_BODY))

            def hidden1(c):
                for m in range(H1 // P):
                    dve.wait_ge(h1_hi_made, c * 4 + m + 1)
                    dve.tensor_tensor(h1_lo[:, c % 2, m, :], h1_raw[:, c % 2, m, :], h1_hi[:, c % 2, m, :].bitcast(F32), op=ALU.subtract)\
                       .then_inc(h1_lo_made, 1)

            split_piece(len(PIECE_UNITS))
            for c in range(CHUNKS):
                hidden1(c)
                if c + 2 < CHUNKS:
                    split_piece(len(PIECE_UNITS) + c + 1)

            dve.wait_ge(l3_done, 1)
            for c in range(CHUNKS):
                dve.tensor_copy(y_sb[32 * c:32 * c + 1, :], z_ps[32 * c:32 * c + 1, :]).then_inc(y_made, 1)


def pair_index(i, j):
    return i * (FIELDS - 1) - i * (i - 1) // 2 + (j - i - 1)


def kernel(**inputs):
    import concourse.bacc as bacc
    from concourse.bass_utils import run_bass_kernel_spmd

    k_in = np.asarray(inputs["L0_rec_kernel"])
    kern = np.zeros((D, K_WIDTH), k_in.dtype)
    w1_in = np.asarray(inputs["W_top1"])
    w1 = np.zeros_like(w1_in)
    for q, (j, k) in enumerate(GROUPS):
        for h in range(2):
            row = z_row(q) + h
            if 2 * k + h < j:
                n = pair_index(2 * k + h, j)
                kern[:, k_col(q) + h * D:k_col(q) + (h + 1) * D] = k_in[:, n]
                w1[row] = w1_in[n]
            else:
                w1[row] = w1_in[FIELDS * (FIELDS - 1) // 2 + k]

    arrays = {
        "ids": np.ascontiguousarray(inputs["ids"]),
        "dense_t": np.ascontiguousarray(np.asarray(inputs["dense_ctx"]).T),
        "kern": np.ascontiguousarray(kern.reshape(D, K_LOADS, 2, K_COLS).transpose(1, 2, 0, 3)).reshape(K_LOADS, P, K_COLS),
        "w1": w1,
        "b1": np.ascontiguousarray(np.asarray(inputs["b_top1"]).reshape(-1, P).T).reshape(-1),
        "w2": np.ascontiguousarray(inputs["W_top2"]),
        "b2": np.ascontiguousarray(np.asarray(inputs["b_top2"]).reshape(-1, P).T).reshape(-1),
        "w3": np.ascontiguousarray(np.asarray(inputs["W_top3"]).reshape(-1, P).T).reshape(-1),
    }
    for f in range(FIELDS):
        arrays[f"tbl_{f}"] = np.ascontiguousarray(inputs[f"tbl_{f}"])

    nc = bacc.Bacc("TRN2", target_bir_lowering=False, num_devices=1)
    ap = {n: nc.dram_tensor(n, a.shape, mybir.dt.from_np(a.dtype), kind="ExternalInput").ap()
          for n, a in arrays.items()}
    out = nc.dram_tensor("y", (B, 1), F32, kind="ExternalOutput").ap()
    build(nc, ap["ids"], ap["dense_t"], [ap[f"tbl_{f}"] for f in range(FIELDS)], ap["kern"],
          ap["w1"], ap["b1"], ap["w2"], ap["b2"], ap["w3"], out)
    r = run_bass_kernel_spmd(nc, [arrays], core_ids=[0])
    return r.results[0]["y"]
```
